# Optimizing a Trainium2 kernel written in Bass

```python
import numpy as np
import jax
import jax.numpy as jnp

def _softmax(x, axis=-1):
    return jax.nn.softmax(x, axis=axis)
def _gelu(x):
    return jax.nn.gelu(x, approximate=True)
def _silu(x):
    return jax.nn.silu(x)
def _sigmoid(x):
    return jax.nn.sigmoid(x)
def _layernorm(x, axis=-1, eps=1e-5):
    m = jnp.mean(x, axis=axis, keepdims=True)
    v = jnp.var(x, axis=axis, keepdims=True)
    return (x - m) / jnp.sqrt(v + eps)
def _scatter_add(tgt, idx, src, axis=0):
    return tgt.at[idx].add(src)
def _segment_sum(src, seg, n):
    return jax.ops.segment_sum(src, seg, n)

kernel_name = 'mk_conv_seq_d1_conv_nchw256_86b073'

def setup_inputs(seed: int = 0):
    np.random.seed(seed)
    _w = jnp.asarray
    def _rec_inputs():
        import jax
        import jax.numpy as jnp
        _gk = jax.random.key(seed)
        x = -0.0002091 + 1 * jax.random.normal(jax.random.fold_in(_gk, 1), (32, 256, 56, 56), jnp.float32)
        return x
    x = _rec_inputs()
    def _L0_conv_setup():
        import jax, jax.numpy as jnp
        import numpy as np
        EPS = 1e-05

        @jax.custom_vjp
        def binarize(x):
            return jnp.where(x >= 0, 1.0, -1.0).astype(x.dtype)

        def _bin_fwd(x):
            return (binarize(x), x)

        def _bin_bwd(x, g):
            return (g * (jnp.abs(x) <= 1.0).astype(g.dtype),)
        binarize.defvjp(_bin_fwd, _bin_bwd)

        def bconv3x3(x, w, stride=1):
            bx = binarize(x)
            bw = binarize(w)
            return jax.lax.conv_general_dilated(bx, bw, window_strides=(stride, stride), padding=[(1, 1), (1, 1)], dimension_numbers=('NCHW', 'OIHW', 'NCHW'))

        def bn(x, gamma, beta, mean, var):
            inv = gamma / jnp.sqrt(var + EPS)
            return x * inv[None, :, None, None] + (beta - mean * inv)[None, :, None, None]

        def channel_shuffle(x, groups=2):
            b, c, h, w = x.shape
            x = x.reshape(b, groups, c // groups, h, w)
            x = jnp.transpose(x, (0, 2, 1, 3, 4))
            return x.reshape(b, c, h, w)

        def hardtanh(x):
            return jnp.clip(x, -1.0, 1.0)
        key = jax.random.key(seed)
        ks = jax.random.split(key, 13)
        P = 128
        inp = {'x': jax.random.normal(ks[0], (32, 2 * P, 56, 56), jnp.float32), 'w1': jax.random.normal(ks[1], (P, P, 3, 3), jnp.float32) * 0.05, 'w2': jax.random.normal(ks[2], (P, P, 3, 3), jnp.float32) * 0.05, 'bn1_gamma': jax.random.uniform(ks[3], (P,), jnp.float32, 0.5, 1.5), 'bn1_beta': jax.random.normal(ks[4], (P,), jnp.float32) * 0.1, 'bn1_mean': jax.random.normal(ks[5], (P,), jnp.float32), 'bn1_var': jax.random.uniform(ks[6], (P,), jnp.float32, 0.5, 1.5), 'bn2_gamma': jax.random.uniform(ks[7], (P,), jnp.float32, 0.5, 1.5), 'bn2_beta': jax.random.normal(ks[8], (P,), jnp.float32) * 0.1, 'bn2_mean': jax.random.normal(ks[9], (P,), jnp.float32), 'bn2_var': jax.random.uniform(ks[10], (P,), jnp.float32, 0.5, 1.5), 'move0_bias': jax.random.normal(ks[11], (P,), jnp.float32) * 0.01, 'move1_bias': jax.random.normal(ks[12], (P,), jnp.float32) * 0.01}
        return inp
    _L0_conv_all = _L0_conv_setup()
    _L0_conv_in = {k: v for k, v in _L0_conv_all.items() if k in ('w1', 'w2', 'bn1_gamma', 'bn1_beta', 'bn1_mean', 'bn1_var', 'bn2_gamma', 'bn2_beta', 'bn2_mean', 'bn2_var', 'move0_bias', 'move1_bias', )}
    del _L0_conv_all

    return {
        "x": x,
        "L0_conv_w1": _L0_conv_in["w1"],
        "L0_conv_w2": _L0_conv_in["w2"],
        "L0_conv_bn1_gamma": _L0_conv_in["bn1_gamma"],
        "L0_conv_bn1_beta": _L0_conv_in["bn1_beta"],
        "L0_conv_bn1_mean": _L0_conv_in["bn1_mean"],
        "L0_conv_bn1_var": _L0_conv_in["bn1_var"],
        "L0_conv_bn2_gamma": _L0_conv_in["bn2_gamma"],
        "L0_conv_bn2_beta": _L0_conv_in["bn2_beta"],
        "L0_conv_bn2_mean": _L0_conv_in["bn2_mean"],
        "L0_conv_bn2_var": _L0_conv_in["bn2_var"],
        "L0_conv_move0_bias": _L0_conv_in["move0_bias"],
        "L0_conv_move1_bias": _L0_conv_in["move1_bias"],
    }

def reference(x, L0_conv_w1, L0_conv_w2, L0_conv_bn1_gamma, L0_conv_bn1_beta, L0_conv_bn1_mean, L0_conv_bn1_var, L0_conv_bn2_gamma, L0_conv_bn2_beta, L0_conv_bn2_mean, L0_conv_bn2_var, L0_conv_move0_bias, L0_conv_move1_bias):
    import jax
    import jax.numpy as jnp
    def _L0_conv_ref(x, w1, w2, bn1_gamma, bn1_beta, bn1_mean, bn1_var, bn2_gamma, bn2_beta, bn2_mean, bn2_var, move0_bias, move1_bias):
        import jax, jax.numpy as jnp
        import numpy as np
        EPS = 1e-05

        @jax.custom_vjp
        def binarize(x):
            return jnp.where(x >= 0, 1.0, -1.0).astype(x.dtype)

        def _bin_fwd(x):
            return (binarize(x), x)

        def _bin_bwd(x, g):
            return (g * (jnp.abs(x) <= 1.0).astype(g.dtype),)
        binarize.defvjp(_bin_fwd, _bin_bwd)

        def bconv3x3(x, w, stride=1):
            bx = binarize(x)
            bw = binarize(w)
            return jax.lax.conv_general_dilated(bx, bw, window_strides=(stride, stride), padding=[(1, 1), (1, 1)], dimension_numbers=('NCHW', 'OIHW', 'NCHW'))

        def bn(x, gamma, beta, mean, var):
            inv = gamma / jnp.sqrt(var + EPS)
            return x * inv[None, :, None, None] + (beta - mean * inv)[None, :, None, None]

        def channel_shuffle(x, groups=2):
            b, c, h, w = x.shape
            x = x.reshape(b, groups, c // groups, h, w)
            x = jnp.transpose(x, (0, 2, 1, 3, 4))
            return x.reshape(b, c, h, w)

        def hardtanh(x):
            return jnp.clip(x, -1.0, 1.0)
        P = w1.shape[0]
        x_act, x_idle = (x[:, :P], x[:, P:])
        residual = x_act
        out = bn(bconv3x3(x_act, w1, stride=1), bn1_gamma, bn1_beta, bn1_mean, bn1_var)
        out = hardtanh(out + residual)
        x_idle = x_idle + move0_bias[None, :, None, None]
        out = channel_shuffle(jnp.concatenate([out, x_idle], axis=1))
        x_act2, x_idle2 = (out[:, :P], out[:, P:])
        residual = x_act2
        out = bn(bconv3x3(x_act2, w2, stride=1), bn2_gamma, bn2_beta, bn2_mean, bn2_var)
        out = hardtanh(out + residual)
        x_idle2 = x_idle2 + move1_bias[None, :, None, None]
        out = channel_shuffle(jnp.concatenate([out, x_idle2], axis=1))
        return out

    def _gn(v, G=32, eps=1e-5):
        B_, C_, H_, W_ = v.shape
        g = v.reshape(B_, G, C_ // G, H_, W_)
        m = jnp.mean(g, axis=(2, 3, 4), keepdims=True)
        s = jnp.var(g, axis=(2, 3, 4), keepdims=True)
        return ((g - m) / jnp.sqrt(s + eps)).reshape(v.shape)

    def _ln_c(v, eps=1e-6):
        m = jnp.mean(v, axis=1, keepdims=True)
        s = jnp.var(v, axis=1, keepdims=True)
        return (v - m) / jnp.sqrt(s + eps)

    def _ln_t(v, eps=1e-5):
        m = jnp.mean(v, axis=-1, keepdims=True)
        s = jnp.var(v, axis=-1, keepdims=True)
        return (v - m) / jnp.sqrt(s + eps)

    def _to_tokens(v):
        B_, C_, H_, W_ = v.shape
        return v.reshape(B_, C_, H_ * W_).transpose(0, 2, 1)
    def _from_tokens(t, like):
        B_, C_, H_, W_ = like.shape
        return t.transpose(0, 2, 1).reshape(B_, C_, H_, W_)

    x = _L0_conv_ref(x, L0_conv_w1, L0_conv_w2, L0_conv_bn1_gamma, L0_conv_bn1_beta, L0_conv_bn1_mean, L0_conv_bn1_var, L0_conv_bn2_gamma, L0_conv_bn2_beta, L0_conv_bn2_mean, L0_conv_bn2_var, L0_conv_move0_bias, L0_conv_move1_bias)
    return x


_drawn_inputs = setup_inputs


def setup_inputs(seed=0):
    import zlib

    import numpy as np

    out = dict(_drawn_inputs(seed))
    spreads = {}
    factors = {'L0_conv_bn2_beta': 4.816, 'L0_conv_bn2_var': 2.829, 'L0_conv_move1_bias': 8.0}
    for name, (base, spread) in spreads.items():
        noise = np.random.default_rng([zlib.crc32(name.encode()), seed]).standard_normal(out[name].shape)
        drawn = base * np.exp(spread * noise) if base else spread * noise
        out[name] = jnp.asarray(drawn.astype(out[name].dtype))
    for name, factor in factors.items():
        out[name] = (out[name] * factor).astype(out[name].dtype)
    return out
```

```python
import concourse.bass as bass
from concourse import mybir
from contextlib import ExitStack

IMAGES = 32
P = 128
HALF = P // 2
SIDE = 56
PIX = SIDE * SIDE
TAPS = 9
EPS = 1e-5

RADIX = 2047.0
ROUNDER = 1.5 * 2.0 ** 23
HROWS = SIDE // 2
VROWS = HROWS + 2
PITCH = SIDE + 2
CHUNK_ROWS = 7
CHUNKS = HROWS // CHUNK_ROWS
CHUNK = CHUNK_ROWS * SIDE
BANK = 512
HPIX = HROWS * SIDE
SLOTS = 4

GAMMA, BETA, MEAN, VAR, MOVE0, MOVE1 = 0, 2, 4, 6, 8, 9


def steps(fori, head=2, turns=IMAGES // SLOTS - 1):
    for c in range(head):
        yield 0, c
    with fori(0, turns) as it:
        for c in range(head, head + SLOTS):
            yield it, c
    for c in range(head, IMAGES + 2 - SLOTS * turns):
        yield turns, c


def image(it, c):
    if isinstance(it, int) and not 0 <= SLOTS * it + c < IMAGES:
        return None
    return it * SLOTS + c, c % SLOTS, it + c // SLOTS


def binary_block(nc, x, w1, w2, params, out):
    fp32, fp16 = mybir.dt.float32, mybir.dt.float16
    ALU, ACT = mybir.AluOpType, mybir.ActivationFunctionType

    ctx = ExitStack()
    with ctx:
        def sb(name, shape, dt):
            return ctx.enter_context(nc.sbuf_tensor(name, shape, dt))

        def sem(name):
            return ctx.enter_context(nc.semaphore(name))

        act = [sb(f"act{s}", [P, PIX], fp32) for s in range(SLOTS)]
        mix = [sb(f"mix{s}", [P, PIX], fp32) for s in range(SLOTS)]
        idle = [sb(f"idle{s}", [P, PIX], fp32) for s in range(SLOTS)]
        upper = [sb(f"upper{k}", [P, VROWS * SIDE], fp16) for k in (1, 2)]
        lower = [sb(f"lower{k}", [P, VROWS * SIDE], fp16) for k in (1, 2)]
        packed = [sb(f"packed{k}", [P, 2 + VROWS * PITCH + 2], fp16) for k in (1, 2)]
        rounded = [sb(f"rounded{k}", [P, HPIX], fp32) for k in (1, 2)]
        low_conv = [sb(f"low_conv{k}", [P, HPIX], fp16) for k in (1, 2)]
        signs = [sb(f"signs{k}", [P, TAPS * P], fp16) for k in (1, 2)]
        unpack = sb("unpack", [P, P], fp16)
        par = sb("par", [P, 10], fp32)
        t = sb("t", [P, 32], fp32)
        conv = [ctx.enter_context(nc.psum_tensor(f"conv{k}", [P, CHUNKS * BANK], fp32)) for k in (1, 2)]
        raw_w = [act[SLOTS - 1][:, k * TAPS * P:(k + 1) * TAPS * P] for k in (0, 1)]

        sv, ss, sr, sq, inv = (t[:, 2 * k:2 * k + 2] for k in range(5))
        bias, gain, low, high = (t[:, 2 * k:2 * k + 2] for k in range(5, 9))
        shift = t[:, 18:19]
        thresh = t[:, 19:20]
        idle_add = t[:, 20:21]
        mean_inv = t[:, 22:24]
        clip_bias = t[:, 24:26]

        s_par = sem("s_par")
        s_w = sem("s_w")
        s_var = sem("s_var")
        s_sqrt = sem("s_sqrt")
        s_chain = sem("s_chain")
        s_params = sem("s_params")
        s_unpack0 = sem("s_unpack0")
        s_unpack = sem("s_unpack")
        s_signs = sem("s_signs")
        act_in = [sem(f"act_in{s}") for s in range(SLOTS)]
        mix_in = [sem(f"mix_in{s}") for s in range(SLOTS)]
        idle_in = [sem(f"idle_in{s}") for s in range(SLOTS)]
        mix_out = [sem(f"mix_out{s}") for s in range(SLOTS)]
        idle_out = [sem(f"idle_out{s}") for s in range(SLOTS)]
        halves_ready = [sem(f"halves_ready{k}") for k in (1, 2)]
        packed_ready = [sem(f"packed_ready{k}") for k in (1, 2)]
        conv_ready = [sem(f"conv_ready{k}") for k in (1, 2)]
        rounded_ready = [sem(f"rounded_ready{k}") for k in (1, 2)]
        low_ready = [sem(f"low_ready{k}") for k in (1, 2)]
        up_ready = [sem(f"up_ready{k}") for k in (1, 2)]
        low_summed = [sem(f"low_summed{k}") for k in (1, 2)]
        up_summed = [sem(f"up_summed{k}") for k in (1, 2)]
        mix_clipped = sem("mix_clipped")
        idle_clipped = sem("idle_clipped")
        out_clipped = sem("out_clipped")
        idle_final = sem("idle_final")
        out_final = sem("out_final")

        def rows(tile, first, count, pitch=SIDE):
            return tile[:, first * pitch:(first + count) * pitch]

        def bank_view(k):
            return conv[k][:, :].rearrange("p (c n) -> p c n", n=BANK)[:, :, 0:CHUNK]

        def chunk_view(ap):
            return ap.rearrange("p (c n) -> p c n", n=CHUNK)

        block = ctx.enter_context(nc.Block())

        @block.sync
        def _(sp):
            sp.dma_start(par[:, :], params).then_inc(s_par, 16)

            def channels(n, first, count):
                return x[bass.ds(n, 1), first:first + count, :].rearrange("a p n -> (a p) n")

            def load_act(n, slot, turn, reused=True):
                if reused:
                    sp.wait_ge(mix_clipped, n - (SLOTS - 1))
                    sp.wait_ge(idle_clipped, n - (SLOTS - 1))
                sp.dma_start(act[slot][:, :], channels(n, 0, P)).then_inc(act_in[slot], 16)

            def load_idle(n, slot, turn, reused=True):
                if reused:
                    sp.wait_ge(idle_out[slot], turn * 32)
                sp.dma_start(idle[slot][0:HALF, :], channels(n, P + HALF, HALF)).then_inc(idle_in[slot], 16)

            def load_mix(n, slot, turn, reused=True):
                if reused:
                    sp.wait_ge(mix_out[slot], turn * 32)
                sp.dma_start(mix[slot][HALF:P, :], channels(n, P, HALF)).then_inc(mix_in[slot], 16)

            def store(tile, ready, done, n, slot, turn, lanes):
                sp.wait_ge(ready, n + 1)
                for first, channel in lanes:
                    dst = out[bass.ds(n, 1), :, channel, :].rearrange("a j n -> (a j) n")
                    sp.dma_start(dst, tile[slot][first:first + HALF, :]).then_inc(done[slot], 16)

            load_act(*image(0, 0), reused=False)
            for k, w in enumerate((w1, w2)):
                sp.dma_start(raw_w[k], w).then_inc(s_w, 16)
            load_act(*image(0, 1), reused=False)
            load_mix(*image(0, 0), reused=False)
            load_idle(*image(0, 0), reused=False)
            load_idle(*image(0, 1), reused=False)
            for it, c in steps(sp.Fori, head=SLOTS - 1, turns=IMAGES // SLOTS - 2):
                act_next, mix_next, idle_now, mix_now = (image(it, c + d) for d in (2, 1, -1, -2))
                peeled = isinstance(it, int) and it == 0
                if act_next:
                    if peeled and c == 1:
                        sp.wait_ge(s_signs, 1)
                    load_act(*act_next, reused=not peeled or c + 2 >= SLOTS)
                if idle_now:
                    store(idle, idle_final, idle_out, *idle_now, ((0, 3), (HALF, 1)))
                if act_next:
                    load_idle(*act_next, reused=not peeled or c + 2 >= SLOTS)
                if mix_now:
                    store(mix, out_final, mix_out, *mix_now, ((HALF, 2), (0, 0)))
                if mix_next:
                    load_mix(*mix_next, reused=not peeled or c + 1 >= SLOTS)
            for s in range(SLOTS):
                sp.wait_ge(idle_out[s], 32 * (IMAGES // SLOTS))
                sp.wait_ge(mix_out[s], 32 * (IMAGES // SLOTS))

        @block.vector
        def _(dve):
            links = [0]

            def link(ins):
                links[0] += 1
                ins.then_inc(s_chain, 1)
                dve.wait_ge(s_chain, links[0])

            def pack(k, src, thr, n, reused=True):
                if reused:
                    dve.wait_ge(packed_ready[k], n)
                nc.vector.tensor_scalar(rows(upper[k], 1, HROWS + 1), rows(src, 0, HROWS + 1), thr, (RADIX + 1) / 2,
                                        ALU.is_ge, ALU.subtract)
                nc.vector.tensor_scalar(rows(lower[k], 0, HROWS + 1), rows(src, HROWS - 1, HROWS + 1), thr, RADIX,
                                        ALU.is_ge, ALU.mult).then_inc(halves_ready[k], 1)
                dve.wait_ge(halves_ready[k], n + 1)
                if reused:
                    dve.wait_ge(conv_ready[k], n)
                inner = packed[k][:, 2:2 + VROWS * PITCH].rearrange("p (r c) -> p r c", c=PITCH)[:, :, 0:SIDE]
                nc.vector.tensor_tensor(inner, upper[k][:, :].rearrange("p (r c) -> p r c", c=SIDE),
                                        lower[k][:, :].rearrange("p (r c) -> p r c", c=SIDE),
                                        ALU.add).then_inc(packed_ready[k], 1)

            def sum_low(k, tile, n):
                dve.wait_ge(low_ready[k], n + 1)
                nc.vector.scalar_tensor_tensor(out=rows(tile, HROWS, HROWS), in0=low_conv[k][:, :],
                                               scalar=gain[:, k:k + 1], in1=rows(tile, HROWS, HROWS),
                                               op0=ALU.mult, op1=ALU.add).then_inc(low_summed[k], 1)

            def sum_up(k, tile, n):
                dve.wait_ge(up_ready[k], n + 1)
                x_up = chunk_view(rows(tile, 0, HROWS))
                nc.vector.scalar_tensor_tensor(out=x_up, in0=bank_view(k), scalar=gain[:, k:k + 1], in1=x_up,
                                               op0=ALU.mult, op1=ALU.add).then_inc(up_summed[k], 1)

            def clip(k, lanes, dst, src, n, done):
                dve.wait_ge(low_summed[k], n + 1)
                dve.wait_ge(up_summed[k], n + 1)
                nc.vector.tensor_scalar(dst[lanes, :], src[lanes, :], high[lanes, k:k + 1], low[lanes, k:k + 1],
                                        ALU.min, ALU.max).then_inc(done, 1)

            for k in (0, 1):
                nc.vector.memset(rows(upper[k], 0, 1), -RADIX / 2)
                nc.vector.memset(rows(lower[k], VROWS - 1, 1), RADIX / 2)
                ins = nc.vector.memset(packed[k][:, :], 0.0)
            link(ins)

            dve.wait_ge(s_par, 16)
            nc.vector.tensor_scalar(sv, par[:, VAR:VAR + 2], EPS, None, ALU.add).then_inc(s_var, 1)
            dve.wait_ge(act_in[0], 16)
            pack(0, act[0], 0.0, 0, reused=False)
            dve.wait_ge(s_w, 32)
            for k in (0, 1):
                link(nc.vector.tensor_scalar(signs[k][:, :], raw_w[k], 0.0, 2.0, ALU.is_ge, ALU.mult))
                ins = nc.vector.tensor_scalar(signs[k][:, :], signs[k][:, :], 1.0, None, ALU.subtract)
            ins.then_inc(s_signs, 1)
            dve.wait_ge(s_sqrt, 1)
            link(nc.vector.reciprocal(sr, ss))
            link(nc.vector.tensor_tensor(sq, sv, sr, ALU.mult))
            link(nc.vector.tensor_tensor(sr, ss, sq, ALU.add))
            link(nc.vector.tensor_scalar(sq, sr, 0.5, None, ALU.mult))
            link(nc.vector.reciprocal(sr, sq))
            link(nc.vector.tensor_tensor(inv, par[:, GAMMA:GAMMA + 2], sr, ALU.mult))
            link(nc.vector.tensor_tensor(mean_inv, par[:, MEAN:MEAN + 2], inv, ALU.mult))
            link(nc.vector.tensor_tensor(bias, par[:, BETA:BETA + 2], mean_inv, ALU.subtract))
            link(nc.vector.tensor_scalar(gain, inv, 2.0, None, ALU.mult))
            link(nc.vector.tensor_copy(shift[0:HALF, :], bias[0:HALF, 0:1]))
            link(nc.vector.tensor_copy(shift[HALF:P, :], par[HALF:P, MOVE0:MOVE0 + 1]))
            link(nc.vector.tensor_scalar(thresh, shift, -1.0, None, ALU.mult))
            link(nc.vector.tensor_copy(clip_bias[:, 0:1], bias[:, 0:1]))
            link(nc.vector.tensor_tensor(clip_bias[:, 1:2], bias[:, 1:2], shift, ALU.add))
            link(nc.vector.tensor_scalar(low, clip_bias, -1.0, -1.0, ALU.mult, ALU.add))
            link(nc.vector.tensor_scalar(high, clip_bias, -1.0, 1.0, ALU.mult, ALU.add))
            link(nc.vector.tensor_tensor(idle_add[0:HALF, :], par[0:HALF, MOVE0:MOVE0 + 1],
                                         par[0:HALF, MOVE1:MOVE1 + 1], ALU.add))
            nc.vector.tensor_tensor(idle_add[HALF:P, :], bias[HALF:P, 0:1], par[HALF:P, MOVE1:MOVE1 + 1],
                                    ALU.add).then_inc(s_params, 1)
            dve.wait_ge(s_params, 1)

            for it, c in steps(dve.Fori):
                now, before, last, ahead = (image(it, c + d) for d in (0, -1, -2, 1))
                if last:
                    n, slot, turn = last
                    sum_low(1, mix[slot], n)
                    sum_up(1, mix[slot], n)
                if before:
                    n, slot, turn = before
                    dve.wait_ge(mix_in[slot], turn * 16 + 16)
                    dve.wait_ge(mix_clipped, n + 1)
                    pack(1, mix[slot], thresh, n, reused=last is not None)
                if last:
                    n, slot, turn = last
                    clip(1, slice(0, P), mix[slot], mix[slot], n, out_clipped)
                if ahead:
                    n, slot, turn = ahead
                    dve.wait_ge(act_in[slot], turn * 16 + 16)
                    pack(0, act[slot], 0.0, n)
                if now:
                    n, slot, turn = now
                    sum_low(0, act[slot], n)
                    sum_up(0, act[slot], n)
                    dve.wait_ge(mix_in[slot], turn * 16 + 16)
                    clip(0, slice(0, HALF), mix[slot], act[slot], n, mix_clipped)
                    dve.wait_ge(idle_in[slot], turn * 16 + 16)
                    clip(0, slice(HALF, P), idle[slot], act[slot], n, idle_clipped)

        @block.tensor
        def _(pe):
            def taps(k, first, count):
                for tap in range(first, first + count):
                    kh, kw = divmod(tap, 3)
                    for chunk in range(CHUNKS):
                        at = 2 + (chunk * CHUNK_ROWS + kh) * PITCH + kw - 1
                        window = packed[k][:, at:at + CHUNK_ROWS * PITCH].rearrange("p (r c) -> p r c", c=PITCH)
                        ins = nc.tensor.matmul(conv[k][:, chunk * BANK:chunk * BANK + CHUNK],
                                               signs[k][:, tap * P:(tap + 1) * P], window[:, :, 0:SIDE],
                                               start=(tap == 0), stop=(tap == TAPS - 1))
                return ins

            def take_off(k, n):
                pe.wait_ge(low_ready[k], n + 1)
                for chunk in range(CHUNKS):
                    ins = nc.tensor.matmul(conv[k][:, chunk * BANK:chunk * BANK + CHUNK], unpack[:, :],
                                           low_conv[k][:, chunk * CHUNK:(chunk + 1) * CHUNK],
                                           start=False, stop=True, skip_group_check=True)
                ins.then_inc(up_ready[k], 1)

            pe.wait_ge(s_signs, 1)
            pe.wait_ge(s_unpack, 1)
            for it, c in steps(pe.Fori):
                now, before, last = (image(it, c - d) for d in range(3))
                if now:
                    n = now[0]
                    pe.wait_ge(packed_ready[0], n + 1)
                    if before:
                        pe.wait_ge(up_summed[0], n)
                    taps(0, 0, 5)
                if last:
                    take_off(1, last[0])
                if now:
                    taps(0, 5, TAPS - 5).then_inc(conv_ready[0], 1)
                if before:
                    n = before[0]
                    pe.wait_ge(packed_ready[1], n + 1)
                    if last:
                        pe.wait_ge(up_summed[1], n)
                    taps(1, 0, 6)
                if now:
                    take_off(0, now[0])
                if before:
                    taps(1, 6, TAPS - 6).then_inc(conv_ready[1], 1)

        @block.scalar
        def _(act_engine):
            act_engine.wait_ge(s_var, 1)
            nc.scalar.activation(ss, sv, ACT.Sqrt).then_inc(s_sqrt, 1)
            act_engine.wait_ge(s_params, 1)

            def round_low(k, n):
                act_engine.wait_ge(conv_ready[k], n + 1)
                nc.scalar.activation(chunk_view(rounded[k][:, :]), bank_view(k), ACT.Copy, bias=ROUNDER,
                                     scale=1.0 / RADIX).then_inc(rounded_ready[k], 1)

            def narrow_low(k, n, reused):
                act_engine.wait_ge(rounded_ready[k], n + 1)
                if reused:
                    act_engine.wait_ge(low_summed[k], n)
                    act_engine.wait_ge(up_ready[k], n)
                nc.scalar.activation(low_conv[k][:, :], rounded[k][:, :], ACT.Copy, bias=-ROUNDER,
                                     scale=1.0).then_inc(low_ready[k], 1)

            for it, c in steps(act_engine.Fori):
                now, before, last = (image(it, c - d) for d in range(3))
                if now:
                    round_low(0, now[0])
                    narrow_low(0, now[0], before)
                if before:
                    n, slot, turn = before
                    act_engine.wait_ge(idle_in[slot], turn * 16 + 16)
                    act_engine.wait_ge(idle_clipped, n + 1)
                    nc.scalar.activation(idle[slot][:, :], idle[slot][:, :], ACT.Identity,
                                         bias=idle_add).then_inc(idle_final, 1)
                if last:
                    n, slot, turn = last
                    act_engine.wait_ge(out_clipped, n + 1)
                    nc.scalar.activation(mix[slot][:, :], mix[slot][:, :], ACT.Identity,
                                         bias=clip_bias[:, 1:2]).then_inc(out_final, 1)
                if before:
                    round_low(1, before[0])
                    narrow_low(1, before[0], last)

        @block.gpsimd
        def _(pool):
            nc.gpsimd.memset(unpack[:, :], 0.0).then_inc(s_unpack0, 1)
            pool.wait_ge(s_unpack0, 1)
            nc.gpsimd.affine_select(out=unpack[:, :], in_=unpack[:, :], compare_op=ALU.not_equal, fill=-RADIX,
                                    base=0, pattern=[[-1, P]], channel_multiplier=1).then_inc(s_unpack, 1)


def kernel(x, L0_conv_w1, L0_conv_w2, L0_conv_bn1_gamma, L0_conv_bn1_beta, L0_conv_bn1_mean, L0_conv_bn1_var,
           L0_conv_bn2_gamma, L0_conv_bn2_beta, L0_conv_bn2_mean, L0_conv_bn2_var, L0_conv_move0_bias,
           L0_conv_move1_bias):
    import numpy as np
    import concourse.bacc as bacc
    from concourse.bass_utils import run_bass_kernel_spmd

    even, odd = np.arange(0, P, 2), np.arange(1, P, 2)
    order = np.concatenate([even, odd])
    a = [np.asarray(v) for v in (L0_conv_bn1_gamma, L0_conv_bn2_gamma, L0_conv_bn1_beta, L0_conv_bn2_beta,
                                 L0_conv_bn1_mean, L0_conv_bn2_mean, L0_conv_bn1_var, L0_conv_bn2_var)]
    for k in (1, 3, 5, 7):
        a[k] = a[k][order]
    move0, move1 = np.asarray(L0_conv_move0_bias), np.asarray(L0_conv_move1_bias)
    a += [np.concatenate([move0[HALF:], move0[:HALF]]), move1[np.concatenate([odd, even])]]
    arrays = {
        "x": np.ascontiguousarray(np.asarray(x)).reshape(IMAGES, 2 * P, PIX),
        "w1": np.ascontiguousarray(np.asarray(L0_conv_w1).transpose(1, 2, 3, 0)).reshape(P, TAPS * P),
        "w2": np.ascontiguousarray(np.asarray(L0_conv_w2)[order][:, order].transpose(1, 2, 3, 0)).reshape(P, TAPS * P),
        "params": np.ascontiguousarray(np.stack(a, axis=1)),
    }
    nc = bacc.Bacc("TRN2", target_bir_lowering=False, num_devices=1)
    aps = {n: nc.dram_tensor(n, v.shape, mybir.dt.float32, kind="ExternalInput").ap() for n, v in arrays.items()}
    out = nc.dram_tensor("out", (IMAGES, HALF, 4, PIX), mybir.dt.float32, kind="ExternalOutput").ap()
    binary_block(nc, aps["x"], aps["w1"], aps["w2"], aps["params"], out)
    r = run_bass_kernel_spmd(nc, [arrays], core_ids=[0])
    return r.results[0]["out"].reshape(IMAGES, 2 * P, SIDE, SIDE)
```

```python
import concourse.bass as bass
from concourse import mybir
from contextlib import ExitStack

IMAGES = 32
P = 128
HALF = P // 2
SIDE = 56
PIX = SIDE * SIDE
TAPS = 9
EPS = 1e-5

RADIX = 2047.0
ROUNDER = 1.5 * 2.0 ** 23
HROWS = SIDE // 2
VROWS = HROWS + 2
PITCH = SIDE + 2
CHUNK_ROWS = 7
CHUNKS = HROWS // CHUNK_ROWS
CHUNK = CHUNK_ROWS * SIDE
BANK = 512
HPIX = HROWS * SIDE
MAIN_SLOTS = 8
SIDE_SLOTS = 4
AHEAD = 3

GAMMA, BETA, MEAN, VAR, MOVE0, MOVE1 = 0, 2, 4, 6, 8, 9


def steps(fori, unroll, head, turns, count=IMAGES + 3):
    for c in range(head):
        yield 0, c
    with fori(0, turns) as it:
        for c in range(head, head + unroll):
            yield it, c
    for c in range(head, count - unroll * turns):
        yield turns, c


def image(it, c, unroll=MAIN_SLOTS):
    if isinstance(it, int) and not 0 <= unroll * it + c < IMAGES:
        return None
    return it * unroll + c


def main_slot(it, c):
    return c % MAIN_SLOTS, it + c // MAIN_SLOTS


def side_slot(it, c):
    return c % SIDE_SLOTS, it * (MAIN_SLOTS // SIDE_SLOTS) + c // SIDE_SLOTS


def binary_block(nc, x, w1, w2, params, out):
    fp32, fp16 = mybir.dt.float32, mybir.dt.float16
    ALU, ACT = mybir.AluOpType, mybir.ActivationFunctionType

    ctx = ExitStack()
    with ctx:
        def sb(name, shape, dt):
            return ctx.enter_context(nc.sbuf_tensor(name, shape, dt))

        def sem(name):
            return ctx.enter_context(nc.semaphore(name))

        main = [sb(f"main{s}", [P, PIX], fp32) for s in range(MAIN_SLOTS)]
        side = [sb(f"side{s}", [P, PIX], fp32) for s in range(SIDE_SLOTS)]
        upper = [sb(f"upper{k}", [P, VROWS * SIDE], fp16) for k in (1, 2)]
        lower = [sb(f"lower{k}", [P, VROWS * SIDE], fp16) for k in (1, 2)]
        packed = [sb(f"packed{k}", [P, 2 + VROWS * PITCH + 2], fp16) for k in (1, 2)]
        rounded = [sb(f"rounded{k}", [P, HPIX], fp32) for k in (1, 2)]
        low_conv = [sb(f"low_conv{k}", [P, HPIX], fp16) for k in (1, 2)]
        signs = [sb(f"signs{k}", [P, TAPS * P], fp16) for k in (1, 2)]
        unpack = sb("unpack", [P, P], fp16)
        par = sb("par", [P, 10], fp32)
        t = sb("t", [P, 32], fp32)
        conv = [ctx.enter_context(nc.psum_tensor(f"conv{k}", [P, CHUNKS * BANK], fp32)) for k in (1, 2)]
        raw_w = [main[MAIN_SLOTS - 1][:, k * TAPS * P:(k + 1) * TAPS * P] for k in (0, 1)]

        sv, ss, sr, sq, inv = (t[:, 2 * k:2 * k + 2] for k in range(5))
        bias, gain, low, high = (t[:, 2 * k:2 * k + 2] for k in range(5, 9))
        shift = t[:, 18:19]
        thresh = t[:, 19:20]
        side_add = t[:, 20:21]
        mean_inv = t[:, 22:24]
        clip_bias = t[:, 24:26]

        s_par = sem("s_par")
        s_w = sem("s_w")
        s_var = sem("s_var")
        s_sqrt = sem("s_sqrt")
        s_chain = sem("s_chain")
        s_params = sem("s_params")
        s_unpack0 = sem("s_unpack0")
        s_unpack = sem("s_unpack")
        s_signs = sem("s_signs")
        act_in = [sem(f"act_in{s}") for s in range(MAIN_SLOTS)]
        mix_in = [sem(f"mix_in{s}") for s in range(MAIN_SLOTS)]
        main_out = [sem(f"main_out{s}") for s in range(MAIN_SLOTS)]
        side_in = [sem(f"side_in{s}") for s in range(SIDE_SLOTS)]
        side_out = [sem(f"side_out{s}") for s in range(SIDE_SLOTS)]
        halves_ready = [sem(f"halves_ready{k}") for k in (1, 2)]
        packed_ready = [sem(f"packed_ready{k}") for k in (1, 2)]
        conv_ready = [sem(f"conv_ready{k}") for k in (1, 2)]
        rounded_ready = [sem(f"rounded_ready{k}") for k in (1, 2)]
        low_ready = [sem(f"low_ready{k}") for k in (1, 2)]
        up_ready = [sem(f"up_ready{k}") for k in (1, 2)]
        low_summed = [sem(f"low_summed{k}") for k in (1, 2)]
        up_summed = [sem(f"up_summed{k}") for k in (1, 2)]
        clipped = [sem(f"clipped{k}") for k in (1, 2)]
        moved = sem("moved")
        side_added = sem("side_added")
        out_final = sem("out_final")

        def rows(tile, first, count, pitch=SIDE):
            return tile[:, first * pitch:(first + count) * pitch]

        def bank_view(k):
            return conv[k][:, :].rearrange("p (c n) -> p c n", n=BANK)[:, :, 0:CHUNK]

        def chunk_view(ap):
            return ap.rearrange("p (c n) -> p c n", n=CHUNK)

        block = ctx.enter_context(nc.Block())

        @block.sync
        def _(sp):
            sp.dma_start(par[:, :], params).then_inc(s_par, 16)

            def channels(n, first, count):
                return x[bass.ds(n, 1), first:first + count, :].rearrange("a p n -> (a p) n")

            def load_act(it, c, reused=True):
                slot, turn = main_slot(it, c)
                if reused:
                    sp.wait_ge(main_out[slot], turn * 32)
                sp.dma_start(main[slot][:, :], channels(image(it, c), 0, P)).then_inc(act_in[slot], 16)

            def load_side(it, c, reused=True):
                slot, turn = side_slot(it, c)
                if reused:
                    sp.wait_ge(side_out[slot], turn * 32)
                sp.dma_start(side[slot][0:HALF, :], channels(image(it, c), P + HALF, HALF)).then_inc(side_in[slot], 16)

            def load_mix(it, c):
                slot, turn = main_slot(it, c)
                sp.wait_ge(moved, image(it, c) + 1)
                sp.dma_start(main[slot][HALF:P, :], channels(image(it, c), P, HALF)).then_inc(mix_in[slot], 16)

            def store(n, tile, first, channel, done):
                dst = out[bass.ds(n, 1), :, channel, :].rearrange("a j n -> (a j) n")
                sp.dma_start(dst, tile[first:first + HALF, :]).then_inc(done, 16)

            load_act(0, 0, reused=False)
            for k, w in enumerate((w1, w2)):
                sp.dma_start(raw_w[k], w).then_inc(s_w, 16)
            load_act(0, 1, reused=False)
            load_side(0, 0, reused=False)
            for c in range(2, AHEAD):
                load_act(0, c, reused=False)
            for it, c in steps(sp.Fori, MAIN_SLOTS, head=MAIN_SLOTS - AHEAD, turns=3, count=IMAGES + 4):
                peeled = isinstance(it, int) and it == 0
                n = image(it, c - 1)
                if n is not None:
                    slot = side_slot(it, c - 1)[0]
                    load_mix(it, c - 1)
                    store(n, side[slot], HALF, 1, side_out[slot])
                n = image(it, c - 4)
                if n is not None:
                    slot = main_slot(it, c - 4)[0]
                    sp.wait_ge(out_final, n + 1)
                    store(n, main[slot], HALF, 2, main_out[slot])
                    store(n, main[slot], 0, 0, main_out[slot])
                if image(it, c + AHEAD) is not None:
                    if peeled and c + AHEAD == MAIN_SLOTS - 1:
                        sp.wait_ge(s_signs, 1)
                    load_act(it, c + AHEAD, reused=not peeled or c + AHEAD >= MAIN_SLOTS)
                n = image(it, c - 1)
                if n is not None:
                    slot = side_slot(it, c - 1)[0]
                    sp.wait_ge(side_added, n + 1)
                    store(n, side[slot], 0, 3, side_out[slot])
                if image(it, c + 1) is not None:
                    load_side(it, c + 1, reused=not peeled or c + 1 >= SIDE_SLOTS)
            for s in range(SIDE_SLOTS):
                sp.wait_ge(side_out[s], 32 * (IMAGES // SIDE_SLOTS))
            for s in range(MAIN_SLOTS):
                sp.wait_ge(main_out[s], 32 * (IMAGES // MAIN_SLOTS))

        @block.vector
        def _(dve):
            links = [0]

            def link(ins):
                links[0] += 1
                ins.then_inc(s_chain, 1)
                dve.wait_ge(s_chain, links[0])

            def pack(k, src, thr, n, reused=True):
                if reused:
                    dve.wait_ge(packed_ready[k], n)
                nc.vector.tensor_scalar(rows(upper[k], 1, HROWS + 1), rows(src, 0, HROWS + 1), thr, (RADIX + 1) / 2,
                                        ALU.is_ge, ALU.subtract)
                nc.vector.tensor_scalar(rows(lower[k], 0, HROWS + 1), rows(src, HROWS - 1, HROWS + 1), thr, RADIX,
                                        ALU.is_ge, ALU.mult).then_inc(halves_ready[k], 1)
                dve.wait_ge(halves_ready[k], n + 1)
                if reused:
                    dve.wait_ge(conv_ready[k], n)
                inner = packed[k][:, 2:2 + VROWS * PITCH].rearrange("p (r c) -> p r c", c=PITCH)[:, :, 0:SIDE]
                nc.vector.tensor_tensor(inner, upper[k][:, :].rearrange("p (r c) -> p r c", c=SIDE),
                                        lower[k][:, :].rearrange("p (r c) -> p r c", c=SIDE),
                                        ALU.add).then_inc(packed_ready[k], 1)

            def sum_low(k, tile, n):
                dve.wait_ge(low_ready[k], n + 1)
                nc.vector.scalar_tensor_tensor(out=rows(tile, HROWS, HROWS), in0=low_conv[k][:, :],
                                               scalar=gain[:, k:k + 1], in1=rows(tile, HROWS, HROWS),
                                               op0=ALU.mult, op1=ALU.add).then_inc(low_summed[k], 1)

            def sum_up(k, tile, n):
                dve.wait_ge(up_ready[k], n + 1)
                x_up = chunk_view(rows(tile, 0, HROWS))
                nc.vector.scalar_tensor_tensor(out=x_up, in0=bank_view(k), scalar=gain[:, k:k + 1], in1=x_up,
                                               op0=ALU.mult, op1=ALU.add).then_inc(up_summed[k], 1)

            def clip(k, tile, n):
                dve.wait_ge(low_summed[k], n + 1)
                dve.wait_ge(up_summed[k], n + 1)
                nc.vector.tensor_scalar(tile[:, :], tile[:, :], high[:, k:k + 1], low[:, k:k + 1],
                                        ALU.min, ALU.max).then_inc(clipped[k], 1)

            for k in (0, 1):
                nc.vector.memset(rows(upper[k], 0, 1), -RADIX / 2)
                nc.vector.memset(rows(lower[k], VROWS - 1, 1), RADIX / 2)
                ins = nc.vector.memset(packed[k][:, :], 0.0)
            link(ins)

            dve.wait_ge(s_par, 16)
            nc.vector.tensor_scalar(sv, par[:, VAR:VAR + 2], EPS, None, ALU.add).then_inc(s_var, 1)
            dve.wait_ge(act_in[0], 16)
            pack(0, main[0], 0.0, 0, reused=False)
            dve.wait_ge(s_w, 32)
            for k in (0, 1):
                link(nc.vector.tensor_scalar(signs[k][:, :], raw_w[k], 0.0, 2.0, ALU.is_ge, ALU.mult))
                ins = nc.vector.tensor_scalar(signs[k][:, :], signs[k][:, :], 1.0, None, ALU.subtract)
            ins.then_inc(s_signs, 1)
            dve.wait_ge(s_sqrt, 1)
            link(nc.vector.reciprocal(sr, ss))
            link(nc.vector.tensor_tensor(sq, sv, sr, ALU.mult))
            link(nc.vector.tensor_tensor(sr, ss, sq, ALU.add))
            link(nc.vector.tensor_scalar(sq, sr, 0.5, None, ALU.mult))
            link(nc.vector.reciprocal(sr, sq))
            link(nc.vector.tensor_tensor(inv, par[:, GAMMA:GAMMA + 2], sr, ALU.mult))
            link(nc.vector.tensor_tensor(mean_inv, par[:, MEAN:MEAN + 2], inv, ALU.mult))
            link(nc.vector.tensor_tensor(bias, par[:, BETA:BETA + 2], mean_inv, ALU.subtract))
            link(nc.vector.tensor_scalar(gain, inv, 2.0, None, ALU.mult))
            link(nc.vector.tensor_copy(shift[0:HALF, :], bias[0:HALF, 0:1]))
            link(nc.vector.tensor_copy(shift[HALF:P, :], par[HALF:P, MOVE0:MOVE0 + 1]))
            link(nc.vector.tensor_scalar(thresh, shift, -1.0, None, ALU.mult))
            link(nc.vector.tensor_copy(clip_bias[:, 0:1], bias[:, 0:1]))
            link(nc.vector.tensor_tensor(clip_bias[:, 1:2], bias[:, 1:2], shift, ALU.add))
            link(nc.vector.tensor_scalar(low, clip_bias, -1.0, -1.0, ALU.mult, ALU.add))
            link(nc.vector.tensor_scalar(high, clip_bias, -1.0, 1.0, ALU.mult, ALU.add))
            link(nc.vector.tensor_tensor(side_add[0:HALF, :], par[0:HALF, MOVE0:MOVE0 + 1],
                                         par[0:HALF, MOVE1:MOVE1 + 1], ALU.add))
            nc.vector.tensor_tensor(side_add[HALF:P, :], bias[HALF:P, 0:1], par[HALF:P, MOVE1:MOVE1 + 1],
                                    ALU.add).then_inc(s_params, 1)
            dve.wait_ge(s_params, 1)

            for it, c in steps(dve.Fori, MAIN_SLOTS, head=4, turns=3):
                now, before, last, ahead = (image(it, c + d) for d in (0, -2, -3, 1))
                if before is not None:
                    slot, turn = main_slot(it, c - 2)
                    dve.wait_ge(mix_in[slot], turn * 16 + 16)
                    dve.wait_ge(clipped[0], before + 1)
                    pack(1, main[slot], thresh, before, reused=last is not None)
                if last is not None:
                    tile = main[main_slot(it, c - 3)[0]]
                    sum_up(1, tile, last)
                    sum_low(1, tile, last)
                    clip(1, tile, last)
                if ahead is not None:
                    slot, turn = main_slot(it, c + 1)
                    dve.wait_ge(act_in[slot], turn * 16 + 16)
                    pack(0, main[slot], 0.0, ahead)
                if now is not None:
                    tile = main[main_slot(it, c)[0]]
                    sum_up(0, tile, now)
                    sum_low(0, tile, now)
                    clip(0, tile, now)

        @block.tensor
        def _(pe):
            def taps(k, first, count):
                for tap in range(first, first + count):
                    kh, kw = divmod(tap, 3)
                    for chunk in range(CHUNKS):
                        at = 2 + (chunk * CHUNK_ROWS + kh) * PITCH + kw - 1
                        window = packed[k][:, at:at + CHUNK_ROWS * PITCH].rearrange("p (r c) -> p r c", c=PITCH)
                        ins = nc.tensor.matmul(conv[k][:, chunk * BANK:chunk * BANK + CHUNK],
                                               signs[k][:, tap * P:(tap + 1) * P], window[:, :, 0:SIDE],
                                               start=(tap == 0), stop=(tap == TAPS - 1))
                return ins

            def take_off(k, n):
                pe.wait_ge(low_ready[k], n + 1)
                for chunk in range(CHUNKS):
                    ins = nc.tensor.matmul(conv[k][:, chunk * BANK:chunk * BANK + CHUNK], unpack[:, :],
                                           low_conv[k][:, chunk * CHUNK:(chunk + 1) * CHUNK],
                                           start=False, stop=True, skip_group_check=True)
                ins.then_inc(up_ready[k], 1)

            pe.wait_ge(s_signs, 1)
            pe.wait_ge(s_unpack, 1)
            for it, c in steps(pe.Fori, 1, head=3, turns=IMAGES - 3):
                now, before, last = (image(it, c - d, 1) for d in (0, 2, 3))
                if now is not None:
                    pe.wait_ge(packed_ready[0], now + 1)
                    if not isinstance(now, int) or now > 0:
                        pe.wait_ge(up_summed[0], now)
                    taps(0, 0, 5)
                if last is not None:
                    take_off(1, last)
                if now is not None:
                    taps(0, 5, TAPS - 5).then_inc(conv_ready[0], 1)
                if before is not None:
                    pe.wait_ge(packed_ready[1], before + 1)
                    if last is not None:
                        pe.wait_ge(up_summed[1], before)
                    taps(1, 0, 4)
                if now is not None:
                    take_off(0, now)
                if before is not None:
                    taps(1, 4, TAPS - 4).then_inc(conv_ready[1], 1)

        @block.scalar
        def _(act_engine):
            act_engine.wait_ge(s_var, 1)
            nc.scalar.activation(ss, sv, ACT.Sqrt).then_inc(s_sqrt, 1)
            act_engine.wait_ge(s_params, 1)

            def round_low(k, n):
                act_engine.wait_ge(conv_ready[k], n + 1)
                nc.scalar.activation(chunk_view(rounded[k][:, :]), bank_view(k), ACT.Copy, bias=ROUNDER,
                                     scale=1.0 / RADIX).then_inc(rounded_ready[k], 1)

            def narrow_low(k, n, reused):
                act_engine.wait_ge(rounded_ready[k], n + 1)
                if reused:
                    act_engine.wait_ge(low_summed[k], n)
                    act_engine.wait_ge(up_ready[k], n)
                nc.scalar.activation(low_conv[k][:, :], rounded[k][:, :], ACT.Copy, bias=-ROUNDER,
                                     scale=1.0).then_inc(low_ready[k], 1)

            for it, c in steps(act_engine.Fori, MAIN_SLOTS, head=4, turns=3):
                now, leaving, before, last = (image(it, c - d) for d in (0, 1, 2, 3))
                if leaving is not None:
                    slot, turn = side_slot(it, c - 1)
                    tile = main[main_slot(it, c - 1)[0]]
                    act_engine.wait_ge(side_in[slot], turn * 16 + 16)
                    act_engine.wait_ge(clipped[0], leaving + 1)
                    nc.scalar.activation(side[slot][HALF:P, :], tile[HALF:P, :], ACT.Identity,
                                         bias=side_add[HALF:P, :]).then_inc(moved, 1)
                if now is not None:
                    round_low(0, now)
                    narrow_low(0, now, reused=not isinstance(now, int) or now > 0)
                if leaving is not None:
                    nc.scalar.activation(side[slot][0:HALF, :], side[slot][0:HALF, :], ACT.Identity,
                                         bias=side_add[0:HALF, :]).then_inc(side_added, 1)
                if last is not None:
                    tile = main[main_slot(it, c - 3)[0]]
                    act_engine.wait_ge(clipped[1], last + 1)
                    nc.scalar.activation(tile[:, :], tile[:, :], ACT.Identity,
                                         bias=clip_bias[:, 1:2]).then_inc(out_final, 1)
                if before is not None:
                    round_low(1, before)
                    narrow_low(1, before, reused=last is not None)

        @block.gpsimd
        def _(pool):
            nc.gpsimd.memset(unpack[:, :], 0.0).then_inc(s_unpack0, 1)
            pool.wait_ge(s_unpack0, 1)
            nc.gpsimd.affine_select(out=unpack[:, :], in_=unpack[:, :], compare_op=ALU.not_equal, fill=-RADIX,
                                    base=0, pattern=[[-1, P]], channel_multiplier=1).then_inc(s_unpack, 1)


def kernel(x, L0_conv_w1, L0_conv_w2, L0_conv_bn1_gamma, L0_conv_bn1_beta, L0_conv_bn1_mean, L0_conv_bn1_var,
           L0_conv_bn2_gamma, L0_conv_bn2_beta, L0_conv_bn2_mean, L0_conv_bn2_var, L0_conv_move0_bias,
           L0_conv_move1_bias):
    import numpy as np
    import concourse.bacc as bacc
    from concourse.bass_utils import run_bass_kernel_spmd

    even, odd = np.arange(0, P, 2), np.arange(1, P, 2)
    order = np.concatenate([even, odd])
    a = [np.asarray(v) for v in (L0_conv_bn1_gamma, L0_conv_bn2_gamma, L0_conv_bn1_beta, L0_conv_bn2_beta,
                                 L0_conv_bn1_mean, L0_conv_bn2_mean, L0_conv_bn1_var, L0_conv_bn2_var)]
    for k in (1, 3, 5, 7):
        a[k] = a[k][order]
    move0, move1 = np.asarray(L0_conv_move0_bias), np.asarray(L0_conv_move1_bias)
    a += [np.concatenate([move0[HALF:], move0[:HALF]]), move1[np.concatenate([odd, even])]]
    arrays = {
        "x": np.ascontiguousarray(np.asarray(x)).reshape(IMAGES, 2 * P, PIX),
        "w1": np.ascontiguousarray(np.asarray(L0_conv_w1).transpose(1, 2, 3, 0)).reshape(P, TAPS * P),
        "w2": np.ascontiguousarray(np.asarray(L0_conv_w2)[order][:, order].transpose(1, 2, 3, 0)).reshape(P, TAPS * P),
        "params": np.ascontiguousarray(np.stack(a, axis=1)),
    }
    nc = bacc.Bacc("TRN2", target_bir_lowering=False, num_devices=1)
    aps = {n: nc.dram_tensor(n, v.shape, mybir.dt.float32, kind="ExternalInput").ap() for n, v in arrays.items()}
    out = nc.dram_tensor("out", (IMAGES, HALF, 4, PIX), mybir.dt.float32, kind="ExternalOutput").ap()
    binary_block(nc, aps["x"], aps["w1"], aps["w2"], aps["params"], out)
    r = run_bass_kernel_spmd(nc, [arrays], core_ids=[0])
    return r.results[0]["out"].reshape(IMAGES, 2 * P, SIDE, SIDE)
```

```python
import concourse.bass as bass
from concourse import mybir
from contextlib import ExitStack

IMAGES = 32
P = 128
HALF = P // 2
SIDE = 56
PIX = SIDE * SIDE
TAPS = 9
EPS = 1e-5

RADIX = 2047.0
ROUNDER = 1.5 * 2.0 ** 23
HROWS = SIDE // 2
VROWS = HROWS + 2
PITCH = SIDE + 2
CHUNK_ROWS = 7
CHUNKS = HROWS // CHUNK_ROWS
CHUNK = CHUNK_ROWS * SIDE
BANK = 512
HPIX = HROWS * SIDE
MAIN_SLOTS = 8
SIDE_SLOTS = 4
AHEAD = 3
AHEAD_AT_START = 5

GAMMA, BETA, MEAN, VAR, MOVE0, MOVE1 = 0, 2, 4, 6, 8, 9


def steps(fori, unroll, head, turns, count=IMAGES + 3):
    for c in range(head):
        yield 0, c
    with fori(0, turns) as it:
        for c in range(head, head + unroll):
            yield it, c
    for c in range(head, count - unroll * turns):
        yield turns, c


def image(it, c, unroll=MAIN_SLOTS):
    if isinstance(it, int) and not 0 <= unroll * it + c < IMAGES:
        return None
    return it * unroll + c


def main_slot(it, c):
    return c % MAIN_SLOTS, it + c // MAIN_SLOTS


def is_last(n):
    return isinstance(n, int) and n == IMAGES - 1


def in_halves(n):
    return isinstance(n, int) and n >= IMAGES - 2


def ended(n, half=0):
    return n + 1 + half + (n - (IMAGES - 2) if in_halves(n) else 0)


def buffers(k, n):
    if k == 1 and isinstance(n, int) and n == IMAGES - 2:
        return 0, IMAGES
    if k == 1 and is_last(n):
        return 1, IMAGES - 2
    return k, n


def side_slot(it, c):
    return c % SIDE_SLOTS, it * (MAIN_SLOTS // SIDE_SLOTS) + c // SIDE_SLOTS


def binary_block(nc, x, w1, w2, params, out):
    fp32, fp16 = mybir.dt.float32, mybir.dt.float16
    ALU, ACT = mybir.AluOpType, mybir.ActivationFunctionType

    ctx = ExitStack()
    with ctx:
        def sb(name, shape, dt):
            return ctx.enter_context(nc.sbuf_tensor(name, shape, dt))

        def sem(name):
            return ctx.enter_context(nc.semaphore(name))

        main = [sb(f"main{s}", [P, PIX], fp32) for s in range(MAIN_SLOTS)]
        side = [sb(f"side{s}", [P, PIX], fp32) for s in range(SIDE_SLOTS)]
        upper = [sb(f"upper{k}", [P, VROWS * SIDE], fp16) for k in (1, 2)]
        lower = [sb(f"lower{k}", [P, VROWS * SIDE], fp16) for k in (1, 2)]
        packed = [sb(f"packed{k}", [P, 2 + VROWS * PITCH + 2], fp16) for k in (1, 2)]
        rounded = [sb(f"rounded{k}", [P, HPIX], fp32) for k in (1, 2)]
        low_conv = [sb(f"low_conv{k}", [P, HPIX], fp16) for k in (1, 2)]
        signs = [sb(f"signs{k}", [P, TAPS * P], fp16) for k in (1, 2)]
        unpack = sb("unpack", [P, P], fp16)
        par = sb("par", [P, 10], fp32)
        t = sb("t", [P, 32], fp32)
        conv = [ctx.enter_context(nc.psum_tensor(f"conv{k}", [P, CHUNKS * BANK], fp32)) for k in (1, 2)]
        raw_w = [main[MAIN_SLOTS - 1][:, k * TAPS * P:(k + 1) * TAPS * P] for k in (0, 1)]

        sv, ss, sr, sq, inv = (t[:, 2 * k:2 * k + 2] for k in range(5))
        bias, gain, low, high = (t[:, 2 * k:2 * k + 2] for k in range(5, 9))
        shift = t[:, 18:19]
        thresh = t[:, 19:20]
        side_add = t[:, 20:21]
        mean_inv = t[:, 22:24]
        clip_bias = t[:, 24:26]

        s_par = sem("s_par")
        s_w = [sem(f"s_w{k}") for k in (1, 2)]
        s_var = sem("s_var")
        s_sqrt = sem("s_sqrt")
        s_chain = sem("s_chain")
        s_params = sem("s_params")
        s_unpack0 = sem("s_unpack0")
        s_unpack = sem("s_unpack")
        s_signs = [sem(f"s_signs{k}") for k in (1, 2)]
        act_in = [sem(f"act_in{s}") for s in range(MAIN_SLOTS)]
        mix_in = [sem(f"mix_in{s}") for s in range(MAIN_SLOTS)]
        main_out = [sem(f"main_out{s}") for s in range(MAIN_SLOTS)]
        side_in = [sem(f"side_in{s}") for s in range(SIDE_SLOTS)]
        side_out = [sem(f"side_out{s}") for s in range(SIDE_SLOTS)]
        upper_ready = [sem(f"upper_ready{k}") for k in (1, 2)]
        lower_ready = [sem(f"lower_ready{k}") for k in (1, 2)]
        packed_ready = [sem(f"packed_ready{k}") for k in (1, 2)]
        conv_ready = [sem(f"conv_ready{k}") for k in (1, 2)]
        rounded_ready = [sem(f"rounded_ready{k}") for k in (1, 2)]
        low_ready = [sem(f"low_ready{k}") for k in (1, 2)]
        up_ready = [sem(f"up_ready{k}") for k in (1, 2)]
        low_summed = [sem(f"low_summed{k}") for k in (1, 2)]
        up_summed = [sem(f"up_summed{k}") for k in (1, 2)]
        clipped = [sem(f"clipped{k}") for k in (1, 2)]
        moved = sem("moved")
        side_added = sem("side_added")
        out_final = sem("out_final")

        def rows(tile, first, count, pitch=SIDE):
            return tile[:, first * pitch:(first + count) * pitch]

        def bank_view(k):
            return conv[k][:, :].rearrange("p (c n) -> p c n", n=BANK)[:, :, 0:CHUNK]

        def chunk_view(ap):
            return ap.rearrange("p (c n) -> p c n", n=CHUNK)

        block = ctx.enter_context(nc.Block())

        @block.sync
        def _(sp):
            sp.dma_start(par[:, :], params).then_inc(s_par, 16)

            def channels(n, first, count):
                return x[bass.ds(n, 1), first:first + count, :].rearrange("a p n -> (a p) n")

            def load_act(it, c, reused=True):
                slot, turn = main_slot(it, c)
                if reused:
                    sp.wait_ge(main_out[slot], turn * 32)
                sp.dma_start(main[slot][:, :], channels(image(it, c), 0, P)).then_inc(act_in[slot], 16)

            def load_side(it, c, reused=True):
                slot, turn = side_slot(it, c)
                if reused:
                    sp.wait_ge(side_out[slot], turn * 32)
                sp.dma_start(side[slot][0:HALF, :], channels(image(it, c), P + HALF, HALF)).then_inc(side_in[slot], 16)

            def load_mix(it, c):
                slot, turn = main_slot(it, c)
                sp.wait_ge(moved, image(it, c) + 1)
                sp.dma_start(main[slot][HALF:P, :], channels(image(it, c), P, HALF)).then_inc(mix_in[slot], 16)

            def store(n, tile, first, channel, done, row=0, count=SIDE):
                pixels = slice(row * SIDE, (row + count) * SIDE)
                dst = out[bass.ds(n, 1), :, channel, pixels].rearrange("a j n -> (a j) n")
                sp.dma_start(dst, tile[first:first + HALF, pixels]).then_inc(done, 16)

            sp.dma_start(raw_w[0], w1).then_inc(s_w[0], 16)
            load_act(0, 0, reused=False)
            sp.dma_start(raw_w[1], w2).then_inc(s_w[1], 16)
            for c in range(1, AHEAD_AT_START):
                load_act(0, c, reused=False)
                if c <= SIDE_SLOTS // 2:
                    load_side(0, c - 1, reused=False)
            for it, c in steps(sp.Fori, MAIN_SLOTS, head=MAIN_SLOTS - AHEAD, turns=3, count=IMAGES + 4):
                peeled = isinstance(it, int) and it == 0
                leaving, done = image(it, c - 1), image(it, c - 4)
                if leaving is not None:
                    load_mix(it, c - 1)
                ahead = c + AHEAD_AT_START - 1 if peeled and c < MAIN_SLOTS - AHEAD else c + AHEAD
                if image(it, ahead) is not None and not (peeled and c == 0) and not (peeled and c < MAIN_SLOTS - AHEAD and ahead >= MAIN_SLOTS):
                    if peeled and ahead == MAIN_SLOTS - 1:
                        sp.wait_ge(s_signs[0], 1)
                        sp.wait_ge(s_signs[1], 1)
                    load_act(it, ahead, reused=not peeled or ahead >= MAIN_SLOTS)
                if image(it, c + 1) is not None and not (peeled and c + 1 < SIDE_SLOTS // 2):
                    load_side(it, c + 1, reused=not peeled or c + 1 >= SIDE_SLOTS)
                if leaving is not None:
                    slot = side_slot(it, c - 1)[0]
                    store(leaving, side[slot], HALF, 1, side_out[slot])
                if done is not None:
                    slot = main_slot(it, c - 4)[0]
                    parts = ((HROWS, HROWS), (0, HROWS)) if in_halves(done) else ((0, SIDE),)
                    for part, (row, count) in enumerate(parts):
                        sp.wait_ge(out_final, ended(done, part))
                        store(done, main[slot], HALF, 2, main_out[slot], row, count)
                        store(done, main[slot], 0, 0, main_out[slot], row, count)
                if leaving is not None:
                    slot = side_slot(it, c - 1)[0]
                    sp.wait_ge(side_added, leaving + 1)
                    store(leaving, side[slot], 0, 3, side_out[slot])
            for s in range(SIDE_SLOTS):
                sp.wait_ge(side_out[s], 32 * (IMAGES // SIDE_SLOTS))
            for s in range(MAIN_SLOTS):
                sp.wait_ge(main_out[s], 32 * (IMAGES // MAIN_SLOTS + in_halves(IMAGES - MAIN_SLOTS + s)))

        @block.vector
        def _(dve):
            links = [0]

            def link(ins):
                links[0] += 1
                ins.then_inc(s_chain, 1)
                dve.wait_ge(s_chain, links[0])

            def take_upper(k, src, thr, n, reused=True):
                if reused:
                    dve.wait_ge(packed_ready[k], n)
                nc.vector.tensor_scalar(rows(upper[k], 1, HROWS + 1), rows(src, 0, HROWS + 1), thr, (RADIX + 1) / 2,
                                        ALU.is_ge, ALU.subtract).then_inc(upper_ready[k], 1)

            def take_lower(k, src, thr, n, reused=True):
                if reused:
                    dve.wait_ge(packed_ready[k], n)
                nc.vector.tensor_scalar(rows(lower[k], 0, HROWS + 1), rows(src, HROWS - 1, HROWS + 1), thr, RADIX,
                                        ALU.is_ge, ALU.mult).then_inc(lower_ready[k], 1)

            def pack(k, n, reused=True):
                b, users = buffers(k, n)
                dve.wait_ge(upper_ready[k], n + 1)
                dve.wait_ge(lower_ready[k], n + 1)
                if reused:
                    dve.wait_ge(conv_ready[b], users)
                inner = packed[b][:, 2:2 + VROWS * PITCH].rearrange("p (r c) -> p r c", c=PITCH)[:, :, 0:SIDE]
                nc.vector.tensor_tensor(inner, upper[k][:, :].rearrange("p (r c) -> p r c", c=SIDE),
                                        lower[k][:, :].rearrange("p (r c) -> p r c", c=SIDE),
                                        ALU.add).then_inc(packed_ready[k], 1)

            def sum_low(k, tile, n):
                dve.wait_ge(low_ready[k], n + 1)
                nc.vector.scalar_tensor_tensor(out=rows(tile, HROWS, HROWS), in0=low_conv[buffers(k, n)[0]][:, :],
                                               scalar=gain[:, k:k + 1], in1=rows(tile, HROWS, HROWS),
                                               op0=ALU.mult, op1=ALU.add).then_inc(low_summed[k], 1)

            def sum_up(k, tile, n):
                dve.wait_ge(up_ready[k], n + 1)
                x_up = chunk_view(rows(tile, 0, HROWS))
                nc.vector.scalar_tensor_tensor(out=x_up, in0=bank_view(buffers(k, n)[0]), scalar=gain[:, k:k + 1], in1=x_up,
                                               op0=ALU.mult, op1=ALU.add).then_inc(up_summed[k], 1)

            def clip(k, part, *sums):
                for summed, n in sums:
                    dve.wait_ge(summed[k], n + 1)
                nc.vector.tensor_scalar(part, part, high[:, k:k + 1], low[:, k:k + 1],
                                        ALU.min, ALU.max).then_inc(clipped[k], 1)

            for k in (0, 1):
                nc.vector.memset(rows(upper[k], 0, 1), -RADIX / 2)
                nc.vector.memset(rows(lower[k], VROWS - 1, 1), RADIX / 2)
                ins = nc.vector.memset(packed[k][:, :], 0.0)
            link(ins)

            dve.wait_ge(s_par, 16)
            nc.vector.tensor_scalar(sv, par[:, VAR:VAR + 2], EPS, None, ALU.add).then_inc(s_var, 1)
            dve.wait_ge(s_sqrt, 1)
            link(nc.vector.reciprocal(sr, ss))
            link(nc.vector.tensor_tensor(sq, sv, sr, ALU.mult))
            link(nc.vector.tensor_tensor(sr, ss, sq, ALU.add))
            link(nc.vector.tensor_scalar(sq, sr, 0.5, None, ALU.mult))
            link(nc.vector.reciprocal(sr, sq))
            link(nc.vector.tensor_tensor(inv, par[:, GAMMA:GAMMA + 2], sr, ALU.mult))
            link(nc.vector.tensor_tensor(mean_inv, par[:, MEAN:MEAN + 2], inv, ALU.mult))
            link(nc.vector.tensor_tensor(bias, par[:, BETA:BETA + 2], mean_inv, ALU.subtract))
            link(nc.vector.tensor_scalar(gain, inv, 2.0, None, ALU.mult))
            link(nc.vector.tensor_copy(shift[0:HALF, :], bias[0:HALF, 0:1]))
            link(nc.vector.tensor_copy(shift[HALF:P, :], par[HALF:P, MOVE0:MOVE0 + 1]))
            link(nc.vector.tensor_scalar(thresh, shift, -1.0, None, ALU.mult))
            link(nc.vector.tensor_copy(clip_bias[:, 0:1], bias[:, 0:1]))
            link(nc.vector.tensor_tensor(clip_bias[:, 1:2], bias[:, 1:2], shift, ALU.add))
            link(nc.vector.tensor_scalar(low, clip_bias, -1.0, -1.0, ALU.mult, ALU.add))
            link(nc.vector.tensor_scalar(high, clip_bias, -1.0, 1.0, ALU.mult, ALU.add))
            link(nc.vector.tensor_tensor(side_add[0:HALF, :], par[0:HALF, MOVE0:MOVE0 + 1],
                                         par[0:HALF, MOVE1:MOVE1 + 1], ALU.add))
            nc.vector.tensor_tensor(side_add[HALF:P, :], bias[HALF:P, 0:1], par[HALF:P, MOVE1:MOVE1 + 1],
                                    ALU.add).then_inc(s_params, 1)
            dve.wait_ge(s_params, 1)

            def take_signs(k):
                dve.wait_ge(s_w[k], 16)
                link(nc.vector.tensor_scalar(signs[k][:, :], raw_w[k], 0.0, 2.0, ALU.is_ge, ALU.mult))
                nc.vector.tensor_scalar(signs[k][:, :], signs[k][:, :], 1.0, None, ALU.subtract).then_inc(s_signs[k], 1)

            take_signs(0)
            dve.wait_ge(act_in[0], 16)
            take_upper(0, main[0], 0.0, 0, reused=False)
            take_lower(0, main[0], 0.0, 0, reused=False)
            pack(0, 0, reused=False)
            take_signs(1)

            for it, c in steps(dve.Fori, MAIN_SLOTS, head=4, turns=3):
                now, leaving, before, last, ahead = (image(it, c + d) for d in (0, -1, -2, -3, 1))
                if before is not None:
                    slot, turn = main_slot(it, c - 2)
                    dve.wait_ge(mix_in[slot], turn * 16 + 16)
                    dve.wait_ge(clipped[0], before + 1)
                    take_upper(1, main[slot], thresh, before, reused=last is not None)
                if leaving is not None:
                    clip(0, main[main_slot(it, c - 1)[0]][:, :], (low_summed, leaving), (up_summed, leaving))
                if before is not None:
                    take_lower(1, main[slot], thresh, before, reused=last is not None)
                if ahead is not None:
                    slot, turn = main_slot(it, c + 1)
                    dve.wait_ge(act_in[slot], turn * 16 + 16)
                    take_upper(0, main[slot], 0.0, ahead)
                if before is not None:
                    pack(1, before, reused=last is not None)
                if last is not None:
                    tile = main[main_slot(it, c - 3)[0]]
                    if in_halves(last):
                        sum_low(1, tile, last)
                        clip(1, rows(tile, HROWS, HROWS), (low_summed, last))
                        sum_up(1, tile, last)
                        clip(1, rows(tile, 0, HROWS), (up_summed, last))
                        continue
                    sum_up(1, tile, last)
                    sum_low(1, tile, last)
                if ahead is not None:
                    take_lower(0, main[slot], 0.0, ahead)
                if last is not None:
                    clip(1, tile[:, :], (low_summed, last), (up_summed, last))
                if ahead is not None:
                    pack(0, ahead)
                if now is not None:
                    tile = main[main_slot(it, c)[0]]
                    sum_up(0, tile, now)
                    sum_low(0, tile, now)

        @block.tensor
        def _(pe):
            def taps(k, n, first, count):
                b = buffers(k, n)[0]
                for tap in range(first, first + count):
                    kh, kw = divmod(tap, 3)
                    for chunk in range(CHUNKS):
                        at = 2 + (chunk * CHUNK_ROWS + kh) * PITCH + kw - 1
                        window = packed[b][:, at:at + CHUNK_ROWS * PITCH].rearrange("p (r c) -> p r c", c=PITCH)
                        ins = nc.tensor.matmul(conv[b][:, chunk * BANK:chunk * BANK + CHUNK],
                                               signs[k][:, tap * P:(tap + 1) * P], window[:, :, 0:SIDE],
                                               start=(tap == 0), stop=(tap == TAPS - 1))
                return ins

            def take_off(k, n):
                b = buffers(k, n)[0]
                pe.wait_ge(low_ready[k], n + 1)
                for chunk in range(CHUNKS):
                    ins = nc.tensor.matmul(conv[b][:, chunk * BANK:chunk * BANK + CHUNK], unpack[:, :],
                                           low_conv[b][:, chunk * CHUNK:(chunk + 1) * CHUNK],
                                           start=False, stop=True, skip_group_check=True)
                ins.then_inc(up_ready[k], 1)

            pe.wait_ge(s_signs[0], 1)
            pe.wait_ge(s_signs[1], 1)
            pe.wait_ge(s_unpack, 1)
            for it, c in steps(pe.Fori, 1, head=3, turns=IMAGES - 3):
                now, before, last = (image(it, c - d, 1) for d in (0, 2, 3))
                if now is not None:
                    pe.wait_ge(packed_ready[0], now + 1)
                    if not isinstance(now, int) or now > 0:
                        pe.wait_ge(up_summed[0], now)
                    taps(0, now, 0, 5)
                if last is not None and not is_last(before):
                    take_off(1, last)
                if now is not None:
                    taps(0, now, 5, TAPS - 5).then_inc(conv_ready[0], 1)
                if before is not None:
                    pe.wait_ge(packed_ready[1], before + 1)
                    if last is not None:
                        b, users = buffers(1, before)
                        pe.wait_ge(up_summed[b], users)
                    taps(1, before, 0, 4)
                if now is not None:
                    take_off(0, now)
                if is_last(before):
                    take_off(1, last)
                if before is not None:
                    taps(1, before, 4, TAPS - 4).then_inc(conv_ready[1], 1)

        @block.scalar
        def _(act_engine):
            act_engine.wait_ge(s_var, 1)
            nc.scalar.activation(ss, sv, ACT.Sqrt).then_inc(s_sqrt, 1)
            act_engine.wait_ge(s_params, 1)

            def round_low(k, n):
                act_engine.wait_ge(conv_ready[k], n + 1)
                b = buffers(k, n)[0]
                nc.scalar.activation(chunk_view(rounded[b][:, :]), bank_view(b), ACT.Copy, bias=ROUNDER,
                                     scale=1.0 / RADIX).then_inc(rounded_ready[k], 1)

            def narrow_low(k, n, reused):
                act_engine.wait_ge(rounded_ready[k], n + 1)
                b, users = buffers(k, n)
                if reused:
                    act_engine.wait_ge(low_summed[b], users)
                    act_engine.wait_ge(up_ready[b], users)
                nc.scalar.activation(low_conv[b][:, :], rounded[b][:, :], ACT.Copy, bias=-ROUNDER,
                                     scale=1.0).then_inc(low_ready[k], 1)

            for it, c in steps(act_engine.Fori, MAIN_SLOTS, head=4, turns=3):
                now, leaving, before, last = (image(it, c - d) for d in (0, 1, 2, 3))
                if leaving is not None:
                    slot, turn = side_slot(it, c - 1)
                    tile = main[main_slot(it, c - 1)[0]]
                    act_engine.wait_ge(side_in[slot], turn * 16 + 16)
                    act_engine.wait_ge(clipped[0], leaving + 1)
                    nc.scalar.activation(side[slot][HALF:P, :], tile[HALF:P, :], ACT.Identity,
                                         bias=side_add[HALF:P, :]).then_inc(moved, 1)
                if now is not None:
                    round_low(0, now)
                    narrow_low(0, now, reused=not isinstance(now, int) or now > 0)
                if leaving is not None:
                    nc.scalar.activation(side[slot][0:HALF, :], side[slot][0:HALF, :], ACT.Identity,
                                         bias=side_add[0:HALF, :]).then_inc(side_added, 1)
                if last is not None:
                    tile = main[main_slot(it, c - 3)[0]]
                    parts = (rows(tile, HROWS, HROWS), rows(tile, 0, HROWS)) if in_halves(last) else (tile[:, :],)
                    for part, done in enumerate(parts):
                        if part == 1 and is_last(before):
                            round_low(1, before)
                            narrow_low(1, before, reused=True)
                        act_engine.wait_ge(clipped[1], ended(last, part))
                        nc.scalar.activation(done, done, ACT.Identity,
                                             bias=clip_bias[:, 1:2]).then_inc(out_final, 1)
                if before is not None and not is_last(before):
                    round_low(1, before)
                    narrow_low(1, before, reused=last is not None)

        @block.gpsimd
        def _(pool):
            nc.gpsimd.memset(unpack[:, :], 0.0).then_inc(s_unpack0, 1)
            pool.wait_ge(s_unpack0, 1)
            nc.gpsimd.affine_select(out=unpack[:, :], in_=unpack[:, :], compare_op=ALU.not_equal, fill=-RADIX,
                                    base=0, pattern=[[-1, P]], channel_multiplier=1).then_inc(s_unpack, 1)


def kernel(x, L0_conv_w1, L0_conv_w2, L0_conv_bn1_gamma, L0_conv_bn1_beta, L0_conv_bn1_mean, L0_conv_bn1_var,
           L0_conv_bn2_gamma, L0_conv_bn2_beta, L0_conv_bn2_mean, L0_conv_bn2_var, L0_conv_move0_bias,
           L0_conv_move1_bias):
    import numpy as np
    import concourse.bacc as bacc
    from concourse.bass_utils import run_bass_kernel_spmd

    even, odd = np.arange(0, P, 2), np.arange(1, P, 2)
    order = np.concatenate([even, odd])
    a = [np.asarray(v) for v in (L0_conv_bn1_gamma, L0_conv_bn2_gamma, L0_conv_bn1_beta, L0_conv_bn2_beta,
                                 L0_conv_bn1_mean, L0_conv_bn2_mean, L0_conv_bn1_var, L0_conv_bn2_var)]
    for k in (1, 3, 5, 7):
        a[k] = a[k][order]
    move0, move1 = np.asarray(L0_conv_move0_bias), np.asarray(L0_conv_move1_bias)
    a += [np.concatenate([move0[HALF:], move0[:HALF]]), move1[np.concatenate([odd, even])]]
    arrays = {
        "x": np.ascontiguousarray(np.asarray(x)).reshape(IMAGES, 2 * P, PIX),
        "w1": np.ascontiguousarray(np.asarray(L0_conv_w1).transpose(1, 2, 3, 0)).reshape(P, TAPS * P),
        "w2": np.ascontiguousarray(np.asarray(L0_conv_w2)[order][:, order].transpose(1, 2, 3, 0)).reshape(P, TAPS * P),
        "params": np.ascontiguousarray(np.stack(a, axis=1)),
    }
    nc = bacc.Bacc("TRN2", target_bir_lowering=False, num_devices=1)
    aps = {n: nc.dram_tensor(n, v.shape, mybir.dt.float32, kind="ExternalInput").ap() for n, v in arrays.items()}
    out = nc.dram_tensor("out", (IMAGES, HALF, 4, PIX), mybir.dt.float32, kind="ExternalOutput").ap()
    binary_block(nc, aps["x"], aps["w1"], aps["w2"], aps["params"], out)
    r = run_bass_kernel_spmd(nc, [arrays], core_ids=[0])
    return r.results[0]["out"].reshape(IMAGES, 2 * P, SIDE, SIDE)
```
